# Optimizing a Trainium2 kernel written in Bass

```python
import numpy as np
import jax
import jax.numpy as jnp

def _softmax(x, axis=-1):
    return jax.nn.softmax(x, axis=axis)

def _gelu(x):
    return jax.nn.gelu(x, approximate=True)

def _silu(x):
    return jax.nn.silu(x)

def _sigmoid(x):
    return jax.nn.sigmoid(x)

def _layernorm(x, axis=-1, eps=1e-05):
    m = jnp.mean(x, axis=axis, keepdims=True)
    v = jnp.var(x, axis=axis, keepdims=True)
    return (x - m) / jnp.sqrt(v + eps)

def _scatter_add(tgt, idx, src, axis=0):
    return tgt.at[idx].add(src)

def _segment_sum(src, seg, n):
    return jax.ops.segment_sum(src, seg, n)
kernel_name = 'mk_dlrm_tower_d1_rec_r8_87b1d5'

def setup_inputs(seed: int=0):
    np.random.seed(seed)
    _w = jnp.asarray

    def _rec_inputs():
        import jax
        import jax.numpy as jnp
        _tk = jax.random.key(seed)
        dense_ctx = jax.random.normal(jax.random.fold_in(_tk, 190), (512, 16), jnp.float32)
        ids = jnp.stack([jax.random.randint(jax.random.fold_in(_tk, 200 + f), (512,), 0, v, jnp.int32) for f, v in enumerate([12500, 1250, 1000, 1000, 1250, 1000, 1000, 12500, 1000, 125000, 1250, 1250, 1000, 1250, 1250, 125000, 12500, 12500, 125000, 12500, 1000, 1250, 1250, 1000, 1250, 1000, 12500, 1250, 1000, 12500, 1250, 1000, 1250, 1250, 1000, 1000, 1000, 1250, 1250, 1250])], axis=1)
        tbl_0 = 0.05 * jax.random.normal(jax.random.fold_in(_tk, 500 + 0), (12500, 64), jnp.float32)
        tbl_1 = 0.05 * jax.random.normal(jax.random.fold_in(_tk, 500 + 1), (1250, 64), jnp.float32)
        tbl_2 = 0.05 * jax.random.normal(jax.random.fold_in(_tk, 500 + 2), (1000, 64), jnp.float32)
        tbl_3 = 0.05 * jax.random.normal(jax.random.fold_in(_tk, 500 + 3), (1000, 64), jnp.float32)
        tbl_4 = 0.05 * jax.random.normal(jax.random.fold_in(_tk, 500 + 4), (1250, 64), jnp.float32)
        tbl_5 = 0.05 * jax.random.normal(jax.random.fold_in(_tk, 500 + 5), (1000, 64), jnp.float32)
        tbl_6 = 0.05 * jax.random.normal(jax.random.fold_in(_tk, 500 + 6), (1000, 64), jnp.float32)
        tbl_7 = 0.05 * jax.random.normal(jax.random.fold_in(_tk, 500 + 7), (12500, 64), jnp.float32)
        tbl_8 = 0.05 * jax.random.normal(jax.random.fold_in(_tk, 500 + 8), (1000, 64), jnp.float32)
        tbl_9 = 0.05 * jax.random.normal(jax.random.fold_in(_tk, 500 + 9), (125000, 64), jnp.float32)
        tbl_10 = 0.05 * jax.random.normal(jax.random.fold_in(_tk, 500 + 10), (1250, 64), jnp.float32)
        tbl_11 = 0.05 * jax.random.normal(jax.random.fold_in(_tk, 500 + 11), (1250, 64), jnp.float32)
        tbl_12 = 0.05 * jax.random.normal(jax.random.fold_in(_tk, 500 + 12), (1000, 64), jnp.float32)
        tbl_13 = 0.05 * jax.random.normal(jax.random.fold_in(_tk, 500 + 13), (1250, 64), jnp.float32)
        tbl_14 = 0.05 * jax.random.normal(jax.random.fold_in(_tk, 500 + 14), (1250, 64), jnp.float32)
        tbl_15 = 0.05 * jax.random.normal(jax.random.fold_in(_tk, 500 + 15), (125000, 64), jnp.float32)
        tbl_16 = 0.05 * jax.random.normal(jax.random.fold_in(_tk, 500 + 16), (12500, 64), jnp.float32)
        tbl_17 = 0.05 * jax.random.normal(jax.random.fold_in(_tk, 500 + 17), (12500, 64), jnp.float32)
        tbl_18 = 0.05 * jax.random.normal(jax.random.fold_in(_tk, 500 + 18), (125000, 64), jnp.float32)
        tbl_19 = 0.05 * jax.random.normal(jax.random.fold_in(_tk, 500 + 19), (12500, 64), jnp.float32)
        tbl_20 = 0.05 * jax.random.normal(jax.random.fold_in(_tk, 500 + 20), (1000, 64), jnp.float32)
        tbl_21 = 0.05 * jax.random.normal(jax.random.fold_in(_tk, 500 + 21), (1250, 64), jnp.float32)
        tbl_22 = 0.05 * jax.random.normal(jax.random.fold_in(_tk, 500 + 22), (1250, 64), jnp.float32)
        tbl_23 = 0.05 * jax.random.normal(jax.random.fold_in(_tk, 500 + 23), (1000, 64), jnp.float32)
        tbl_24 = 0.05 * jax.random.normal(jax.random.fold_in(_tk, 500 + 24), (1250, 64), jnp.float32)
        tbl_25 = 0.05 * jax.random.normal(jax.random.fold_in(_tk, 500 + 25), (1000, 64), jnp.float32)
        tbl_26 = 0.05 * jax.random.normal(jax.random.fold_in(_tk, 500 + 26), (12500, 64), jnp.float32)
        tbl_27 = 0.05 * jax.random.normal(jax.random.fold_in(_tk, 500 + 27), (1250, 64), jnp.float32)
        tbl_28 = 0.05 * jax.random.normal(jax.random.fold_in(_tk, 500 + 28), (1000, 64), jnp.float32)
        tbl_29 = 0.05 * jax.random.normal(jax.random.fold_in(_tk, 500 + 29), (12500, 64), jnp.float32)
        tbl_30 = 0.05 * jax.random.normal(jax.random.fold_in(_tk, 500 + 30), (1250, 64), jnp.float32)
        tbl_31 = 0.05 * jax.random.normal(jax.random.fold_in(_tk, 500 + 31), (1000, 64), jnp.float32)
        tbl_32 = 0.05 * jax.random.normal(jax.random.fold_in(_tk, 500 + 32), (1250, 64), jnp.float32)
        tbl_33 = 0.05 * jax.random.normal(jax.random.fold_in(_tk, 500 + 33), (1250, 64), jnp.float32)
        tbl_34 = 0.05 * jax.random.normal(jax.random.fold_in(_tk, 500 + 34), (1000, 64), jnp.float32)
        tbl_35 = 0.05 * jax.random.normal(jax.random.fold_in(_tk, 500 + 35), (1000, 64), jnp.float32)
        tbl_36 = 0.05 * jax.random.normal(jax.random.fold_in(_tk, 500 + 36), (1000, 64), jnp.float32)
        tbl_37 = 0.05 * jax.random.normal(jax.random.fold_in(_tk, 500 + 37), (1250, 64), jnp.float32)
        tbl_38 = 0.05 * jax.random.normal(jax.random.fold_in(_tk, 500 + 38), (1250, 64), jnp.float32)
        tbl_39 = 0.05 * jax.random.normal(jax.random.fold_in(_tk, 500 + 39), (1250, 64), jnp.float32)
        _rk = jax.random.fold_in(_tk, 7)
        W_top1 = 0.0354441 * jax.random.normal(jax.random.fold_in(_tk, 801), (796, 512), jnp.float32)
        W_top2 = 0.0441942 * jax.random.normal(jax.random.fold_in(_tk, 802), (512, 256), jnp.float32)
        W_top3 = 0.0625 * jax.random.normal(jax.random.fold_in(_tk, 803), (256, 1), jnp.float32)
        b_top1 = jnp.zeros((512,), jnp.float32)
        b_top2 = jnp.zeros((256,), jnp.float32)
        return (dense_ctx, ids, tbl_0, tbl_1, tbl_2, tbl_3, tbl_4, tbl_5, tbl_6, tbl_7, tbl_8, tbl_9, tbl_10, tbl_11, tbl_12, tbl_13, tbl_14, tbl_15, tbl_16, tbl_17, tbl_18, tbl_19, tbl_20, tbl_21, tbl_22, tbl_23, tbl_24, tbl_25, tbl_26, tbl_27, tbl_28, tbl_29, tbl_30, tbl_31, tbl_32, tbl_33, tbl_34, tbl_35, tbl_36, tbl_37, tbl_38, tbl_39, W_top1, b_top1, W_top2, b_top2, W_top3)
    dense_ctx, ids, tbl_0, tbl_1, tbl_2, tbl_3, tbl_4, tbl_5, tbl_6, tbl_7, tbl_8, tbl_9, tbl_10, tbl_11, tbl_12, tbl_13, tbl_14, tbl_15, tbl_16, tbl_17, tbl_18, tbl_19, tbl_20, tbl_21, tbl_22, tbl_23, tbl_24, tbl_25, tbl_26, tbl_27, tbl_28, tbl_29, tbl_30, tbl_31, tbl_32, tbl_33, tbl_34, tbl_35, tbl_36, tbl_37, tbl_38, tbl_39, W_top1, b_top1, W_top2, b_top2, W_top3 = _rec_inputs()

    def _L0_rec_setup():
        import jax, jax.numpy as jnp
        import numpy as np

        def _pair_indices(num_fields):
            i_idx, j_idx = np.triu_indices(num_fields, k=1)
            return (jnp.asarray(i_idx), jnp.asarray(j_idx))
        key = jax.random.key(seed)
        k1, k2 = jax.random.split(key)
        B, F, D = (256, 40, 64)
        P = F * (F - 1) // 2
        x = jax.random.normal(k1, (B, F, D), dtype=jnp.float32)
        W = jax.random.normal(k2, (P, D, D), dtype=jnp.float32) * (1.0 / np.sqrt(D))
        return {'x': x, 'W': W}
    _L0_rec_all = _L0_rec_setup()
    _L0_rec_in = {k: v for k, v in _L0_rec_all.items() if k in ('W',)}
    del _L0_rec_all
    return {'dense_ctx': dense_ctx, 'ids': ids, 'tbl_0': tbl_0, 'tbl_1': tbl_1, 'tbl_2': tbl_2, 'tbl_3': tbl_3, 'tbl_4': tbl_4, 'tbl_5': tbl_5, 'tbl_6': tbl_6, 'tbl_7': tbl_7, 'tbl_8': tbl_8, 'tbl_9': tbl_9, 'tbl_10': tbl_10, 'tbl_11': tbl_11, 'tbl_12': tbl_12, 'tbl_13': tbl_13, 'tbl_14': tbl_14, 'tbl_15': tbl_15, 'tbl_16': tbl_16, 'tbl_17': tbl_17, 'tbl_18': tbl_18, 'tbl_19': tbl_19, 'tbl_20': tbl_20, 'tbl_21': tbl_21, 'tbl_22': tbl_22, 'tbl_23': tbl_23, 'tbl_24': tbl_24, 'tbl_25': tbl_25, 'tbl_26': tbl_26, 'tbl_27': tbl_27, 'tbl_28': tbl_28, 'tbl_29': tbl_29, 'tbl_30': tbl_30, 'tbl_31': tbl_31, 'tbl_32': tbl_32, 'tbl_33': tbl_33, 'tbl_34': tbl_34, 'tbl_35': tbl_35, 'tbl_36': tbl_36, 'tbl_37': tbl_37, 'tbl_38': tbl_38, 'tbl_39': tbl_39, 'W_top1': W_top1, 'b_top1': b_top1, 'W_top2': W_top2, 'b_top2': b_top2, 'W_top3': W_top3, 'L0_rec_W': _L0_rec_in['W']}

def reference(dense_ctx, ids, tbl_0, tbl_1, tbl_2, tbl_3, tbl_4, tbl_5, tbl_6, tbl_7, tbl_8, tbl_9, tbl_10, tbl_11, tbl_12, tbl_13, tbl_14, tbl_15, tbl_16, tbl_17, tbl_18, tbl_19, tbl_20, tbl_21, tbl_22, tbl_23, tbl_24, tbl_25, tbl_26, tbl_27, tbl_28, tbl_29, tbl_30, tbl_31, tbl_32, tbl_33, tbl_34, tbl_35, tbl_36, tbl_37, tbl_38, tbl_39, W_top1, b_top1, W_top2, b_top2, W_top3, L0_rec_W):
    import jax
    import jax.numpy as jnp

    def _L0_rec_ref(x, W):
        import jax, jax.numpy as jnp
        import numpy as np

        def _pair_indices(num_fields):
            i_idx, j_idx = np.triu_indices(num_fields, k=1)
            return (jnp.asarray(i_idx), jnp.asarray(j_idx))
        B, F, D = x.shape
        i_idx, j_idx = _pair_indices(F)
        vi = x[:, i_idx, :]
        vj = x[:, j_idx, :]
        viW = jnp.einsum('bpd,pde->bpe', vi, W)
        out = jnp.einsum('bpe,bpe->bp', viW, vj)
        return out
    e = jnp.stack([tbl_0[ids[:, 0]], tbl_1[ids[:, 1]], tbl_2[ids[:, 2]], tbl_3[ids[:, 3]], tbl_4[ids[:, 4]], tbl_5[ids[:, 5]], tbl_6[ids[:, 6]], tbl_7[ids[:, 7]], tbl_8[ids[:, 8]], tbl_9[ids[:, 9]], tbl_10[ids[:, 10]], tbl_11[ids[:, 11]], tbl_12[ids[:, 12]], tbl_13[ids[:, 13]], tbl_14[ids[:, 14]], tbl_15[ids[:, 15]], tbl_16[ids[:, 16]], tbl_17[ids[:, 17]], tbl_18[ids[:, 18]], tbl_19[ids[:, 19]], tbl_20[ids[:, 20]], tbl_21[ids[:, 21]], tbl_22[ids[:, 22]], tbl_23[ids[:, 23]], tbl_24[ids[:, 24]], tbl_25[ids[:, 25]], tbl_26[ids[:, 26]], tbl_27[ids[:, 27]], tbl_28[ids[:, 28]], tbl_29[ids[:, 29]], tbl_30[ids[:, 30]], tbl_31[ids[:, 31]], tbl_32[ids[:, 32]], tbl_33[ids[:, 33]], tbl_34[ids[:, 34]], tbl_35[ids[:, 35]], tbl_36[ids[:, 36]], tbl_37[ids[:, 37]], tbl_38[ids[:, 38]], tbl_39[ids[:, 39]]], axis=1)
    z = _L0_rec_ref(e, L0_rec_W)
    z = z.reshape(z.shape[0], -1)
    h = jnp.concatenate([z, dense_ctx], axis=1)
    h = jnp.maximum(h @ W_top1 + b_top1, 0.0)
    h = jnp.maximum(h @ W_top2 + b_top2, 0.0)
    y = h @ W_top3
    return y

_drawn_inputs = setup_inputs


def setup_inputs(seed=0):
    import zlib

    import numpy as np

    out = dict(_drawn_inputs(seed))
    spreads = {'b_top1': (0.0, 0.1), 'b_top2': (0.0, 0.1)}
    factors = {'tbl_0': 2.694}
    for name, (base, spread) in spreads.items():
        noise = np.random.default_rng([zlib.crc32(name.encode()), seed]).standard_normal(out[name].shape)
        drawn = base * np.exp(spread * noise) if base else spread * noise
        out[name] = jnp.asarray(drawn.astype(out[name].dtype))
    for name, factor in factors.items():
        out[name] = (out[name] * factor).astype(out[name].dtype)
    return out
```

```python
from contextlib import ExitStack

import numpy as np

import concourse.bass as bass
from concourse import mybir

F32 = mybir.dt.float32
F32R = mybir.dt.float32r
I32 = mybir.dt.int32
ALU = mybir.AluOpType
ACT = mybir.ActivationFunctionType

P = 128
BATCH = 512
BT = BATCH // P
FIELDS = 40
DIM = 64
DENSE = 16
PAIRS = FIELDS * (FIELDS - 1) // 2
KP = FIELDS // 2
SP_ = KP // 2
H1, H2 = 512, 256

BLOCKS = 4
PER_CHUNK = 16
X_RING = 4
G_RING = 4
W_RING = 6
RAW_RING = 4
P_RING = 3
DVE_SPLITS = 30
LAG = 1
STEPS = 3
LOOK = 4


def pair(i, j):
    return i * FIELDS - i * (i + 1) // 2 + j - i - 1


def plan_groups():
    groups = []
    for k in reversed(range(KP)):
        for M in range(k // 2 + 1, SP_):
            groups.append((k, [(i, (pair(i, 2 * m), pair(i, 2 * m + 1)), m)
                               for m in (2 * M, 2 * M + 1) for i in (2 * k, 2 * k + 1)]))
        if k % 2 == 0:
            own = [(2 * c, (None, pair(2 * c, 2 * c + 1)), c) for c in (k, k + 1)]
            cross = [(i, (pair(i, 2 * k + 2), pair(i, 2 * k + 3)), k + 1) for i in (2 * k, 2 * k + 1)]
            groups.append((k, own + cross))
    return groups


GROUPS = plan_groups()
NG = len(GROUPS)
CHUNKS = -(-NG // PER_CHUNK)
LAST_ROWS = 2 * (NG - PER_CHUNK * (CHUNKS - 1))
DENSE_AT = 32 * (BLOCKS - 1) + LAST_ROWS


AHEAD = 3
LATE = 1


def arrival(k):
    return KP - 1 - k


def first_group(u):
    return next((n for n, (k, _) in enumerate(GROUPS) if arrival(k) >= u), NG)


def last_use(u):
    return first_group(u + 1 if u % 2 else u + 2) - 1


def loads_of_turn(u):
    at = [min(RAW_RING + first_group(v) // 2, NG // 2) for v in (u, u + 1)]
    return range(*at)


def order():
    yield "fields", 0
    for u in range(KP):
        a, b = first_group(u), first_group(u + 1)
        early = b if u < LATE else max(a, b - AHEAD)
        for n in range(a, b + 1):
            if n == early and u + 1 < KP:
                yield "fields", u + 1
            if n < b:
                yield "group", n


def tower_kernel(nc, w_groups, ids, tables, dense, w1, b1, w2, b2, w3, out):
    with ExitStack() as ctx:
        def sb(name, shape, dt=F32):
            return ctx.enter_context(nc.sbuf_tensor(name, shape, dt))

        def ps(name, shape, dt=F32):
            return ctx.enter_context(nc.psum_tensor(name, shape, dt))

        def sem(name):
            return ctx.enter_context(nc.semaphore(name))

        ids_sb = sb("ids_sb", [P, FIELDS * BT], I32)
        ident = sb("ident", [P, P])
        halves = sb("halves", [P, 2 * (2 * PER_CHUNK - 1)])
        rows = sb("rows", [P, G_RING, BT, 2 * DIM])
        E = sb("E", [P, KP, BATCH])
        parts = sb("parts", [P, 2, 2, BATCH], F32R)
        x = sb("x", [P, X_RING, 2, 2, BATCH], F32R)
        w_raw = sb("w_raw", [P, RAW_RING, 2, BLOCKS * P])
        w_hl = sb("w_hl", [P, W_RING, BLOCKS * P], F32R)
        prod = sb("prod", [P, P_RING, BLOCKS, BATCH])
        z = sb("z", [P, CHUNKS, BATCH])
        w1_sb = sb("w1_sb", [P, CHUNKS, H1])
        w2_sb = sb("w2_sb", [P, H1 // P, H2])
        w3_sb = sb("w3_sb", [P, H2 // P])
        b1_sb = sb("b1_sb", [P, H1 // P])
        b2_sb = sb("b2_sb", [P, H2 // P])
        y_sb = sb("y_sb", [1, BATCH])
        h1 = E[:, 0:H1 // P, :]
        h2 = E[:, H1 // P:H1 // P + H2 // P, :]

        ps_t = ps("ps_t", [P, STEPS, 2, BATCH])
        ps_e = ps("ps_e", [P, BATCH])
        ps_z = ps("ps_z", [P, BATCH])
        free = [(2 * NG + s) % STEPS for s in range(STEPS)]
        h1_bank = [ps_e[:], ps_t[:, free[0], 0, :], ps_t[:, free[0], 1, :], ps_t[:, free[1], 0, :]]
        h2_bank = [ps_t[:, free[1], 1, :], ps_t[:, free[2], 0, :]]
        y_bank = ps_t[:, free[2], 1, :]

        ids_loaded = sem("ids_loaded")
        params_loaded = sem("params_loaded")
        ident_zeroed = sem("ident_zeroed")
        ident_ready = sem("ident_ready")
        halves_zeroed = sem("halves_zeroed")
        halves_ready = sem("halves_ready")
        rows_loaded = [sem(f"rows_loaded{i}") for i in range(G_RING)]
        transposed = sem("transposed")
        e_copied = sem("e_copied")
        high_ready = sem("high_ready")
        low_ready = sem("low_ready")
        x_loaded = [sem(f"x_loaded{i}") for i in range(X_RING)]
        raw_loaded = [sem(f"raw_loaded{i}") for i in range(RAW_RING)]
        w_high_ready = sem("w_high_ready")
        w_split_dve = sem("w_split_dve")
        w_split_pool = sem("w_split_pool")
        step_done = sem("step_done")
        product_ready = sem("product_ready")
        group_reduced = sem("group_reduced")
        z_copied = sem("z_copied")
        z_tail_copied = sem("z_tail_copied")
        h1_summed = sem("h1_summed")
        h1_ready = sem("h1_ready")
        h2_summed = sem("h2_summed")
        h2_ready = sem("h2_ready")
        y_summed = sem("y_summed")
        y_ready = sem("y_ready")
        stored = sem("stored")

        def wait_split(eng, n):
            if n < DVE_SPLITS:
                eng.wait_ge(w_split_dve, n + 1)
            else:
                eng.wait_ge(w_split_pool, n + 1 - DVE_SPLITS)

        def wait_rows(eng, u):
            eng.wait_ge(rows_loaded[u % G_RING], 16 * 2 * BT * (u // G_RING + 1))

        def split_low(eng, n):
            low = w_hl[DIM:P, n % W_RING, :]
            eng.wait_ge(w_high_ready, n + 1)
            eng.tensor_tensor(low, w_raw[DIM:P, n // 2 % RAW_RING, n % 2, :], low, ALU.subtract).then_inc(
                w_split_dve if n < DVE_SPLITS else w_split_pool, 1)

        block = ctx.enter_context(nc.Block())

        @block.sync
        def _(sp):
            sp.dma_start(ids_sb[:], ids).then_inc(ids_loaded, 16)

            def load_weights(r):
                if r >= RAW_RING:
                    wait_split(sp, 2 * (r - RAW_RING) + 1)
                for half in (0, DIM):
                    sp.dma_start(w_raw[half:half + DIM, r % RAW_RING, :, :],
                                 w_groups[r]).then_inc(raw_loaded[r % RAW_RING], 16)

            def spread_parts(u):
                if u >= X_RING:
                    sp.wait_ge(step_done, 2 * last_use(u - X_RING) + 2)
                sp.wait_ge(high_ready, u + 1)
                sp.wait_ge(low_ready, u + 1)
                for f in range(2):
                    for half in (0, DIM):
                        sp.dma_start(x[half:half + DIM, u % X_RING, f, :, :].bitcast(F32),
                                     parts[f * DIM:(f + 1) * DIM, u % 2, :, :].bitcast(F32)).then_inc(
                                         x_loaded[u % X_RING], 16)

            loads = iter(range(NG // 2))
            for _ in range(RAW_RING):
                load_weights(next(loads))
            for u in range(KP):
                spread_parts(u)
                if u == 1:
                    for c in range(CHUNKS - 1):
                        sp.dma_start(w1_sb[:, c, :], w1[c]).then_inc(params_loaded, 16)
                    sp.dma_start(w1_sb[:, CHUNKS - 1, :], w1[CHUNKS - 1]).then_inc(params_loaded, 16)
                    sp.dma_start(z[DENSE_AT:DENSE_AT + DENSE, CHUNKS - 1, :], dense).then_inc(params_loaded, 16)
                    sp.dma_start(w2_sb[:], w2).then_inc(params_loaded, 16)
                    sp.dma_start(w3_sb[:], w3).then_inc(params_loaded, 16)
                    sp.dma_start(b1_sb[:], b1).then_inc(params_loaded, 16)
                    sp.dma_start(b2_sb[:], b2).then_inc(params_loaded, 16)
                for r in loads_of_turn(u):
                    load_weights(r)
            sp.wait_ge(y_ready, 1)
            sp.dma_start(out, y_sb[:]).then_inc(stored, 16)
            sp.wait_ge(stored, 16)

        @block.gpsimd
        def _(pool):
            pool.memset(ident[:], 0.0).then_inc(ident_zeroed, 1)
            pool.wait_ge(ident_zeroed, 1)
            pool.affine_select(out=ident[:], in_=ident[:], compare_op=ALU.not_equal, fill=1.0, base=0,
                               pattern=[[-1, P]], channel_multiplier=1).then_inc(ident_ready, 1)
            pool.wait_ge(ids_loaded, 16)

            def gather(u):
                k = KP - 1 - u
                if u >= G_RING:
                    pool.wait_ge(transposed, u - G_RING + 1)
                for f in range(2):
                    for b in range(BT):
                        col = (2 * k + f) * BT + b
                        pool.indirect_dma_start(
                            rows[:, u % G_RING, b, f * DIM:(f + 1) * DIM], None, tables[2 * k + f],
                            bass.IndirectOffsetOnAxis(ap=ids_sb[:, col:col + 1], axis=0),
                        ).then_inc(rows_loaded[u % G_RING], 16)

            for u in range(G_RING):
                gather(u)
            gathered = G_RING
            for u in range(KP):
                for n in range(first_group(u), first_group(u + 1)):
                    if n == first_group(u) + (first_group(u + 1) - first_group(u)) // 2 and gathered < KP:
                        if n + LOOK > DVE_SPLITS:
                            pool.wait_ge(w_split_pool, n + LOOK - DVE_SPLITS)
                        gather(gathered)
                        gathered += 1
                    if DVE_SPLITS <= n + LOOK < NG:
                        wait_rows(pool, gathered - 1)
                        split_low(pool, n + LOOK)
                if first_group(u) == first_group(u + 1):
                    gather(gathered)
                    gathered += 1

        @block.scalar
        def _(act):
            def high_weights(n):
                act.wait_ge(raw_loaded[n // 2 % RAW_RING], 32 * (n // 2 // RAW_RING + 1))
                if n >= W_RING:
                    act.wait_ge(step_done, 2 * (n - W_RING) + 2)
                act.activation(w_hl[:, n % W_RING, :], w_raw[:, n // 2 % RAW_RING, n % 2, :],
                               ACT.Copy).then_inc(w_high_ready, 1)

            def split_fields(u):
                act.wait_ge(transposed, u + 1)
                act.activation(E[:, KP - 1 - u, :], ps_e[:], ACT.Copy).then_inc(e_copied, 1)
                if u >= 2:
                    act.wait_ge(x_loaded[(u - 2) % X_RING], 64 * ((u - 2) // X_RING + 1))
                act.activation(parts[:, u % 2, 0, :], ps_e[:], ACT.Copy).then_inc(high_ready, 1)

            def copy_z(c):
                if c < CHUNKS - 1:
                    act.wait_ge(group_reduced, PER_CHUNK * (c + 1))
                    act.activation(z[:, c, :], ps_z[:], ACT.Copy).then_inc(z_copied, 1)
                else:
                    act.wait_ge(group_reduced, NG)
                    top = 32 * (BLOCKS - 1)
                    act.activation(z[0:top, c, :], ps_z[0:top, :], ACT.Copy).then_inc(z_copied, 1)

            for n in range(LOOK):
                high_weights(n)
            for kind, at in order():
                if kind == "fields":
                    split_fields(at)
                elif kind == "group":
                    if at + LOOK < NG:
                        high_weights(at + LOOK)
                    if at >= LAG and (at - LAG) % PER_CHUNK == PER_CHUNK - 1:
                        copy_z((at - LAG) // PER_CHUNK)
            copy_z(CHUNKS - 1)
            act.wait_ge(params_loaded, 16 * (CHUNKS + 5))
            for m in range(H1 // P):
                act.wait_ge(h1_summed, m + 1)
                act.activation(h1[:, m, :], h1_bank[m], ACT.Relu, bias=b1_sb[:, m:m + 1]).then_inc(h1_ready, 1)
            for m in range(H2 // P):
                act.wait_ge(h2_summed, m + 1)
                act.activation(h2[:, m, :], h2_bank[m], ACT.Relu, bias=b2_sb[:, m:m + 1]).then_inc(h2_ready, 1)
            act.wait_ge(y_summed, 1)
            act.activation(y_sb[:], y_bank[0:1, :], ACT.Copy).then_inc(y_ready, 1)

        @block.vector
        def _(dve):
            dve.memset(halves[:], 0.0).then_inc(halves_zeroed, 1)
            mid = 2 * (PER_CHUNK - 1)
            dve.wait_ge(halves_zeroed, 1)
            dve.memset(halves[0:DIM, mid:mid + 1], 1.0).then_inc(halves_ready, 1)
            dve.memset(halves[DIM:P, mid + 1:mid + 2], 1.0).then_inc(halves_ready, 1)

            def low_fields(u):
                dve.wait_ge(high_ready, u + 1)
                dve.tensor_tensor(parts[:, u % 2, 1, :], ps_e[:], parts[:, u % 2, 0, :],
                                  ALU.subtract).then_inc(low_ready, 1)

            def multiply(n):
                slot = n % P_RING
                if n >= P_RING:
                    dve.wait_ge(group_reduced, n - P_RING + 1)
                blocks = GROUPS[n][1]
                for s in range(2):
                    m0, m1 = blocks[2 * s][2], blocks[2 * s + 1][2]
                    dve.wait_ge(e_copied, arrival(min(m0, m1)) + 1)
                    dve.wait_ge(step_done, 2 * n + s + 1)
                    if m0 == m1:
                        multiplier = E[:, m0, None, :].to_broadcast([P, 2, BATCH])
                    else:
                        multiplier = E[:, m0:m0 + 2, :]
                    dve.tensor_tensor(prod[:, slot, 2 * s:2 * s + 2, :], ps_t[:, (2 * n + s) % STEPS, :, :], multiplier,
                                      ALU.mult).then_inc(product_ready, 1)

            for n in range(LOOK):
                split_low(dve, n)
            for kind, at in order():
                if kind == "fields":
                    low_fields(at)
                else:
                    if at + LOOK < DVE_SPLITS:
                        split_low(dve, at + LOOK)
                    multiply(at)
            dve.wait_ge(group_reduced, NG)
            top = 32 * (BLOCKS - 1)
            dve.tensor_copy(z[top:top + LAST_ROWS, CHUNKS - 1, :],
                            ps_z[top:top + LAST_ROWS, :]).then_inc(z_tail_copied, 1)

        @block.tensor
        def _(pe):
            def transpose_fields(u):
                wait_rows(pe, u)
                if u >= 1:
                    pe.wait_ge(low_ready, u)
                for b in range(BT):
                    last = pe.transpose(ps_e[:, b * P:(b + 1) * P], rows[:, u % G_RING, b, :], ident[:])
                last.then_inc(transposed, 1)

            def products(n):
                wait_split(pe, n)
                k, blocks = GROUPS[n]
                for s in range(2):
                    step = 2 * n + s
                    if step >= STEPS:
                        pe.wait_ge(product_ready, step - STEPS + 1)
                    for j in range(2):
                        b = 2 * s + j
                        i = blocks[b][0]
                        u = arrival(i // 2)
                        pe.wait_ge(x_loaded[u % X_RING], 64 * (u // X_RING + 1))
                        for part in range(2):
                            last = pe.matmul(ps_t[:, step % STEPS, j, :], w_hl[:, n % W_RING, b * P:(b + 1) * P],
                                             x[:, u % X_RING, i % 2, part, :],
                                             start=(part == 0), stop=(part == 1))
                    last.then_inc(step_done, 1)

            def reduce(n):
                pe.wait_ge(product_ready, 2 * n + 2)
                c, q = divmod(n, PER_CHUNK)
                if c >= 1 and q == 0:
                    pe.wait_ge(z_copied, c)
                at = 2 * (PER_CHUNK - 1 - q)
                for b in range(BLOCKS):
                    last = pe.matmul(ps_z[32 * b:32 * b + 32, :], halves[:, at:at + 32],
                                     prod[:, n % P_RING, b, :], start=(q == 0),
                                     stop=(q == PER_CHUNK - 1 or n == NG - 1))
                last.then_inc(group_reduced, 1)

            pe.wait_ge(ident_ready, 1)
            pe.wait_ge(halves_ready, 2)
            for kind, at in order():
                if kind == "fields":
                    transpose_fields(at)
                else:
                    products(at)
                    if at >= LAG:
                        reduce(at - LAG)

            for n in range(NG - LAG, NG - 1):
                reduce(n)
            pe.wait_ge(params_loaded, 16 * (CHUNKS + 5))
            pe.wait_ge(z_copied, CHUNKS - 1)
            pe.wait_ge(low_ready, KP)

            def sum_h1(m, c0, c1):
                for c in range(c0, c1):
                    used = DENSE_AT + DENSE if c == CHUNKS - 1 else P
                    last = pe.matmul(h1_bank[m], w1_sb[0:used, c, m * P:(m + 1) * P], z[0:used, c, :],
                                     start=(c == 0), stop=(c == CHUNKS - 1))
                return last

            for m in range(3):
                sum_h1(m, 0, CHUNKS - 1)
            reduce(NG - 1)
            for m in range(3, H1 // P):
                sum_h1(m, 0, CHUNKS - 1)
            pe.wait_ge(z_copied, CHUNKS)
            pe.wait_ge(z_tail_copied, 1)
            for m in range(H1 // P):
                sum_h1(m, CHUNKS - 1, CHUNKS).then_inc(h1_summed, 1)
            for c in range(H1 // P):
                pe.wait_ge(h1_ready, c + 1)
                for m in range(H2 // P):
                    last = pe.matmul(h2_bank[m], w2_sb[:, c, m * P:(m + 1) * P], h1[:, c, :],
                                     start=(c == 0), stop=(c == H1 // P - 1))
                    if c == H1 // P - 1:
                        last.then_inc(h2_summed, 1)
            for c in range(H2 // P):
                pe.wait_ge(h2_ready, c + 1)
                last = pe.matmul(y_bank[0:1, :], w3_sb[:, c:c + 1], h2[:, c, :],
                                 start=(c == 0), stop=(c == H2 // P - 1))
            last.then_inc(y_summed, 1)


def z_rows():
    at = np.full((CHUNKS, P), -1)
    for n, (_, blocks) in enumerate(GROUPS):
        for b, (_, halves, _) in enumerate(blocks):
            for h, p in enumerate(halves):
                if p is not None:
                    at[n // PER_CHUNK, 32 * b + 2 * (n % PER_CHUNK) + h] = p
    at[CHUNKS - 1, DENSE_AT:DENSE_AT + DENSE] = PAIRS + np.arange(DENSE)
    return at


def kernel(**inputs):
    from concourse import bacc
    from concourse.bass_utils import run_bass_kernel_spmd

    a = {k: np.asarray(v) for k, v in inputs.items()}
    f32 = a["L0_rec_W"].dtype

    w = np.concatenate([a["L0_rec_W"], np.zeros((1, DIM, DIM), f32)])
    rows = [[[PAIRS if p is None else p for p in halves] for _, halves, _ in blocks] for _, blocks in GROUPS]
    w_groups = w[np.array(rows).reshape(NG // 2, 2, BLOCKS, 2)].transpose(0, 4, 1, 2, 3, 5)
    w1 = np.concatenate([a["W_top1"], np.zeros((1, H1), f32)])[z_rows()]
    arrays = {
        "w_groups": w_groups.reshape(NG // 2, DIM, 2, BLOCKS * P),
        "ids_t": a["ids"].reshape(BT, P, FIELDS).transpose(1, 2, 0).reshape(P, FIELDS * BT),
        "dense_t": a["dense_ctx"].T,
        "w1": w1,
        "b1": a["b_top1"].reshape(H1 // P, P).T,
        "w2": a["W_top2"].reshape(H1 // P, P, H2).transpose(1, 0, 2),
        "b2": a["b_top2"].reshape(H2 // P, P).T,
        "w3": a["W_top3"].reshape(H2 // P, P).T,
    }
    for f in range(FIELDS):
        arrays[f"tbl_{f}"] = a[f"tbl_{f}"]
    arrays = {f"in_{k}": np.ascontiguousarray(v) for k, v in arrays.items()}

    nc = bacc.Bacc("TRN2", target_bir_lowering=False, num_devices=1)
    ap = {k: nc.dram_tensor(k, v.shape, mybir.dt.from_np(v.dtype), kind="ExternalInput").ap()
          for k, v in arrays.items()}
    out = nc.dram_tensor("out_y", (1, BATCH), F32, kind="ExternalOutput").ap()
    tower_kernel(nc, ap["in_w_groups"], ap["in_ids_t"], [ap[f"in_tbl_{f}"] for f in range(FIELDS)],
                 ap["in_dense_t"], ap["in_w1"], ap["in_b1"], ap["in_w2"], ap["in_b2"], ap["in_w3"], out)
    r = run_bass_kernel_spmd(nc, [arrays], core_ids=[0])
    return r.results[0]["out_y"].reshape(BATCH, 1)
```

```python
from contextlib import ExitStack

import numpy as np

import concourse.bass as bass
from concourse import mybir

F32 = mybir.dt.float32
F32R = mybir.dt.float32r
I32 = mybir.dt.int32
ALU = mybir.AluOpType
ACT = mybir.ActivationFunctionType

P = 128
BATCH = 512
BT = BATCH // P
FIELDS = 40
DIM = 64
DENSE = 16
PAIRS = FIELDS * (FIELDS - 1) // 2
KP = FIELDS // 2
SP_ = KP // 2
H1, H2 = 512, 256

BLOCKS = 4
PER_CHUNK = 16
X_RING = 4
LOOKED_UP = 2
CODE_RING = 4
G_RING = 4
W_RING = 4
RAW_RING = 4
P_RING = 3
DVE_SPLITS = 50
LAG = 1
STEPS = 3
LOOK = 3


def pair(i, j):
    return i * FIELDS - i * (i + 1) // 2 + j - i - 1


def plan_groups():
    groups = []
    for k in reversed(range(KP)):
        for M in range(k // 2 + 1, SP_):
            groups.append((k, [(i, (pair(i, 2 * m), pair(i, 2 * m + 1)), m)
                               for m in (2 * M, 2 * M + 1) for i in (2 * k, 2 * k + 1)]))
        if k % 2 == 0:
            own = [(2 * c, (None, pair(2 * c, 2 * c + 1)), c) for c in (k, k + 1)]
            cross = [(i, (pair(i, 2 * k + 2), pair(i, 2 * k + 3)), k + 1) for i in (2 * k, 2 * k + 1)]
            groups.append((k, own + cross))
    return groups


GROUPS = plan_groups()
NG = len(GROUPS)
NU = NG // 2
CHUNKS = -(-NG // PER_CHUNK)
LAST_ROWS = 2 * (NG - PER_CHUNK * (CHUNKS - 1))
DENSE_AT = 32 * (BLOCKS - 1) + LAST_ROWS


AHEAD = 5
PARAMS_AT = 12


def arrival(k):
    return KP - 1 - k


def first_group(u):
    return next((n for n, (k, _) in enumerate(GROUPS) if arrival(k) >= u), NG)


def last_use(u):
    return first_group(u + 1 if u % 2 else u + 2) - 1


def order():
    u = 0
    for n in range(NG):
        while u < KP and first_group(u) - AHEAD <= n:
            yield "fields", u
            u += 1
        yield "group", n


def table_split(rows):
    used = max(d for d in range(1, P + 1) if rows % d == 0)
    return used, rows // used


def tower_kernel(nc, w_units, ids, ids_by_field, tables, dense, w1, b1, w2, b2, w3, out):
    with ExitStack() as ctx:
        def sb(name, shape, dt=F32):
            return ctx.enter_context(nc.sbuf_tensor(name, shape, dt))

        def ps(name, shape, dt=F32):
            return ctx.enter_context(nc.psum_tensor(name, shape, dt))

        def sem(name):
            return ctx.enter_context(nc.semaphore(name))

        ids_sb = sb("ids_sb", [P, FIELDS * BT], I32)
        ident = sb("ident", [P, P])
        looked_up = [2 * (KP - 1 - u) + f for u in range(LOOKED_UP) for f in range(2)]
        splits = {f: table_split(tables[f].shape[0]) for f in looked_up}
        small = {f: sb(f"small_{f}", [splits[f][0], splits[f][1], DIM]) for f in looked_up}
        ids_wide = sb("ids_wide", [P, len(looked_up), BATCH], I32)
        first_row = sb("first_row", [P, len(looked_up)], I32)
        first_row_f = sb("first_row_f", [P, len(looked_up)])
        codes = sb("codes", [P, CODE_RING, BATCH])
        halves = sb("halves", [P, 2 * (2 * PER_CHUNK - 1)])
        rows = sb("rows", [P, G_RING, BT, 2 * DIM])
        E = sb("E", [P, KP, BATCH])
        parts = sb("parts", [P, 2, 2, BATCH], F32R)
        x = sb("x", [P, X_RING, 2, 2, BATCH], F32R)
        w_raw = sb("w_raw", [P, RAW_RING, 2 * BLOCKS // 2 * P])
        w_high = sb("w_high", [P, 2, 2 * BLOCKS // 2 * P], F32R)
        w_low = sb("w_low", [P, 2, 2 * BLOCKS // 2 * P], F32R)
        w_hl = sb("w_hl", [P, W_RING, 2, 2 * BLOCKS // 2 * P], F32R)
        prod = sb("prod", [P, P_RING, BLOCKS, BATCH])
        z = sb("z", [P, CHUNKS, BATCH])
        w1_sb = sb("w1_sb", [P, CHUNKS, H1])
        w2_sb = sb("w2_sb", [P, H1 // P, H2])
        w3_sb = sb("w3_sb", [P, H2 // P])
        b1_sb = sb("b1_sb", [P, H1 // P])
        b2_sb = sb("b2_sb", [P, H2 // P])
        y_sb = sb("y_sb", [1, BATCH])
        h1 = E[:, 0:H1 // P, :]
        h2 = E[:, H1 // P:H1 // P + H2 // P, :]

        ps_t = ps("ps_t", [P, STEPS, 2, BATCH])
        ps_e = ps("ps_e", [P, BATCH])
        ps_z = ps("ps_z", [P, BATCH])
        free = [(2 * NG + s) % STEPS for s in range(STEPS)]
        h1_bank = [ps_e[:], ps_t[:, free[0], 0, :], ps_t[:, free[0], 1, :], ps_t[:, free[1], 0, :]]
        h2_bank = [ps_t[:, free[1], 1, :], ps_t[:, free[2], 0, :]]
        y_bank = ps_t[:, free[2], 1, :]
        e_bank = [ps_e[:], ps_t[:, STEPS - 1, 0, :], ps_t[:, STEPS - 1, 1, :]] + [ps_e[:]] * (KP - 3)

        ids_loaded = sem("ids_loaded")
        params_loaded = sem("params_loaded")
        wide_loaded = sem("wide_loaded")
        small_loaded = {f: sem(f"small_loaded{f}") for f in looked_up}
        first_row_ready = sem("first_row_ready")
        first_row_cast = sem("first_row_cast")
        code_ready = sem("code_ready")
        code_used = sem("code_used")
        ident_zeroed = sem("ident_zeroed")
        ident_ready = sem("ident_ready")
        halves_zeroed = sem("halves_zeroed")
        halves_ready = sem("halves_ready")
        rows_loaded = [sem(f"rows_loaded{i}") for i in range(G_RING)]
        transposed = sem("transposed")
        e_copied = sem("e_copied")
        high_ready = sem("high_ready")
        low_ready = sem("low_ready")
        x_loaded = [sem(f"x_loaded{i}") for i in range(X_RING)]
        raw_loaded = [sem(f"raw_loaded{i}") for i in range(RAW_RING)]
        w_high_ready = sem("w_high_ready")
        w_high_placed = sem("w_high_placed")
        w_low_dve = sem("w_low_dve")
        w_low_pool = sem("w_low_pool")
        w_low_placed = [sem(f"w_low_placed{i}") for i in range(W_RING)]
        step_done = sem("step_done")
        product_ready = sem("product_ready")
        group_reduced = sem("group_reduced")
        z_copied = sem("z_copied")
        z_tail_copied = sem("z_tail_copied")
        h1_summed = sem("h1_summed")
        h1_ready = sem("h1_ready")
        h2_summed = sem("h2_summed")
        h2_ready = sem("h2_ready")
        y_summed = sem("y_summed")
        y_ready = sem("y_ready")
        stored = sem("stored")

        code_list = [[(f, c) for c in range(max(splits[f][1] for f in looked_up[2 * u:2 * u + 2]))
                      for f in looked_up[2 * u:2 * u + 2] if c < splits[f][1]] for u in range(LOOKED_UP)]

        def wait_low(eng, m):
            if m < DVE_SPLITS:
                eng.wait_ge(w_low_dve, m + 1)
            else:
                eng.wait_ge(w_low_pool, m + 1 - DVE_SPLITS)

        def wait_rows(eng, u):
            g = u - LOOKED_UP
            eng.wait_ge(rows_loaded[g % G_RING], 16 * 2 * BT * (g // G_RING + 1))

        def low_weights(eng, m):
            eng.wait_ge(w_high_ready, m + 1)
            if m >= 2:
                eng.wait_ge(w_low_placed[(m - 2) % W_RING], 32 * ((m - 2) // W_RING + 1))
            eng.tensor_tensor(w_low[:, m % 2, :], w_raw[:, m % RAW_RING, :], w_high[:, m % 2, :],
                              ALU.subtract).then_inc(w_low_dve if m < DVE_SPLITS else w_low_pool, 1)

        block = ctx.enter_context(nc.Block())

        @block.sync
        def _(sp):
            sp.dma_start(ids_sb[:], ids).then_inc(ids_loaded, 16)
            low = min(looked_up)
            sp.dma_start(ids_wide[:], ids_by_field[None, low:low + len(looked_up), :].to_broadcast(
                [P, len(looked_up), BATCH])).then_inc(wide_loaded, 16)
            for f in looked_up:
                sp.dma_start(small[f][:], tables[f].rearrange("(p c) n -> p c n", p=splits[f][0])).then_inc(
                    small_loaded[f], 16)

            def load_params():
                for c in range(CHUNKS):
                    sp.dma_start(w1_sb[:, c, :], w1[c]).then_inc(params_loaded, 16)
                sp.dma_start(z[DENSE_AT:DENSE_AT + DENSE, CHUNKS - 1, :], dense).then_inc(params_loaded, 16)
                sp.dma_start(w2_sb[:], w2).then_inc(params_loaded, 16)
                sp.dma_start(w3_sb[:], w3).then_inc(params_loaded, 16)
                sp.dma_start(b1_sb[:], b1).then_inc(params_loaded, 16)
                sp.dma_start(b2_sb[:], b2).then_inc(params_loaded, 16)

            def load_weights(m):
                if m >= RAW_RING:
                    wait_low(sp, m - RAW_RING)
                    sp.wait_ge(w_high_placed, 2 * (m - RAW_RING) + 2)
                sp.dma_start(w_raw[:, m % RAW_RING, :], w_units[m]).then_inc(raw_loaded[m % RAW_RING], 16)

            def place_low(m):
                wait_low(sp, m)
                if m >= W_RING:
                    sp.wait_ge(step_done, 4 * (m - W_RING) + 4)
                for odd, (src, dst) in enumerate(((0, DIM), (DIM, 0))):
                    sp.dma_start(w_hl[dst:dst + DIM, m % W_RING, odd, :].bitcast(F32),
                                 w_low[src:src + DIM, m % 2, :].bitcast(F32)).then_inc(
                                     w_low_placed[m % W_RING], 16)

            def spread_parts(u):
                if u >= X_RING:
                    sp.wait_ge(step_done, 2 * last_use(u - X_RING) + 2)
                sp.wait_ge(high_ready, u + 1)
                sp.wait_ge(low_ready, u + 1)
                for f in range(2):
                    for half in (0, DIM):
                        sp.dma_start(x[half:half + DIM, u % X_RING, f, :, :].bitcast(F32),
                                     parts[f * DIM:(f + 1) * DIM, u % 2, :, :].bitcast(F32)).then_inc(
                                         x_loaded[u % X_RING], 16)

            for m in range(RAW_RING):
                load_weights(m)
            for m in range(LOOK):
                place_low(m)
                load_weights(m + RAW_RING)
            for kind, at in order():
                if kind == "fields":
                    spread_parts(at)
                    if at == PARAMS_AT:
                        load_params()
                elif at % 2 == 0 and at // 2 + LOOK < NU:
                    place_low(at // 2 + LOOK)
                    if at // 2 + LOOK + RAW_RING < NU:
                        load_weights(at // 2 + LOOK + RAW_RING)
            sp.wait_ge(y_ready, 1)
            sp.dma_start(out, y_sb[:]).then_inc(stored, 16)
            sp.wait_ge(stored, 16)

        @block.gpsimd
        def _(pool):
            pool.memset(ident[:], 0.0).then_inc(ident_zeroed, 1)
            pool.wait_ge(ident_zeroed, 1)
            pool.affine_select(out=ident[:], in_=ident[:], compare_op=ALU.not_equal, fill=1.0, base=0,
                               pattern=[[-1, P]], channel_multiplier=1).then_inc(ident_ready, 1)
            for i, f in enumerate(looked_up):
                pool.iota(first_row[:, i:i + 1], pattern=[[0, 1]], base=0,
                          channel_multiplier=splits[f][1]).then_inc(first_row_ready, 1)
            pool.wait_ge(ids_loaded, 16)

            def gather(u):
                k = KP - 1 - u
                g = u - LOOKED_UP
                if g >= G_RING:
                    pool.wait_ge(transposed, g - G_RING + 1)
                for f in range(2):
                    for b in range(BT):
                        col = (2 * k + f) * BT + b
                        pool.indirect_dma_start(
                            rows[:, g % G_RING, b, f * DIM:(f + 1) * DIM], None, tables[2 * k + f],
                            bass.IndirectOffsetOnAxis(ap=ids_sb[:, col:col + 1], axis=0),
                        ).then_inc(rows_loaded[g % G_RING], 16)

            for u in range(LOOKED_UP, KP):
                gather(u)

        @block.scalar
        def _(act):
            def high_weights(m):
                act.wait_ge(raw_loaded[m % RAW_RING], 16 * (m // RAW_RING + 1))
                if m >= 2:
                    wait_low(act, m - 2)
                act.activation(w_high[:, m % 2, :], w_raw[:, m % RAW_RING, :], ACT.Copy).then_inc(w_high_ready, 1)
                if m >= W_RING:
                    act.wait_ge(step_done, 4 * (m - W_RING) + 4)
                for odd, at in enumerate((0, DIM)):
                    act.activation(w_hl[at:at + DIM, m % W_RING, odd, :], w_raw[at:at + DIM, m % RAW_RING, :],
                                   ACT.Copy).then_inc(w_high_placed, 1)

            def split_fields(u):
                if u < LOOKED_UP:
                    act.wait_ge(code_used, sum(len(codes_of) for codes_of in code_list[:u + 1]))
                else:
                    act.wait_ge(transposed, u - LOOKED_UP + 1)
                act.activation(E[:, KP - 1 - u, :], e_bank[u], ACT.Copy).then_inc(e_copied, 1)
                if u >= 2:
                    act.wait_ge(x_loaded[(u - 2) % X_RING], 64 * ((u - 2) // X_RING + 1))
                act.activation(parts[:, u % 2, 0, :], e_bank[u], ACT.Copy).then_inc(high_ready, 1)

            def copy_z(c):
                if c < CHUNKS - 1:
                    act.wait_ge(group_reduced, PER_CHUNK * (c + 1))
                    act.activation(z[:, c, :], ps_z[:], ACT.Copy).then_inc(z_copied, 1)
                else:
                    act.wait_ge(group_reduced, NG)
                    top = 32 * (BLOCKS - 1)
                    act.activation(z[0:top, c, :], ps_z[0:top, :], ACT.Copy).then_inc(z_copied, 1)

            for m in range(LOOK):
                high_weights(m)
            for kind, at in order():
                if kind == "fields":
                    split_fields(at)
                elif kind == "group":
                    if at % 2 == 0 and at // 2 + LOOK < NU:
                        high_weights(at // 2 + LOOK)
                    if at >= LAG and (at - LAG) % PER_CHUNK == PER_CHUNK - 1:
                        copy_z((at - LAG) // PER_CHUNK)
            copy_z(CHUNKS - 1)
            act.wait_ge(params_loaded, 16 * (CHUNKS + 5))
            for m in range(H1 // P):
                act.wait_ge(h1_summed, m + 1)
                act.activation(h1[:, m, :], h1_bank[m], ACT.Relu, bias=b1_sb[:, m:m + 1]).then_inc(h1_ready, 1)
            for m in range(H2 // P):
                act.wait_ge(h2_summed, m + 1)
                act.activation(h2[:, m, :], h2_bank[m], ACT.Relu, bias=b2_sb[:, m:m + 1]).then_inc(h2_ready, 1)
            act.wait_ge(y_summed, 1)
            act.activation(y_sb[:], y_bank[0:1, :], ACT.Copy).then_inc(y_ready, 1)

        @block.vector
        def _(dve):
            dve.memset(halves[:], 0.0).then_inc(halves_zeroed, 1)
            mid = 2 * (PER_CHUNK - 1)
            dve.wait_ge(halves_zeroed, 1)
            dve.memset(halves[0:DIM, mid:mid + 1], 1.0).then_inc(halves_ready, 1)
            dve.memset(halves[DIM:P, mid + 1:mid + 2], 1.0).then_inc(halves_ready, 1)

            low = min(looked_up)
            dve.wait_ge(first_row_ready, len(looked_up))
            dve.tensor_copy(first_row_f[:], first_row[:]).then_inc(first_row_cast, 1)
            dve.wait_ge(first_row_cast, 1)
            dve.wait_ge(wide_loaded, 16)

            def low_fields(u):
                dve.wait_ge(high_ready, u + 1)
                dve.tensor_tensor(parts[:, u % 2, 1, :], e_bank[u], parts[:, u % 2, 0, :],
                                  ALU.subtract).then_inc(low_ready, 1)

            weights_split = 0

            def encode(u):
                nonlocal weights_split
                """One-hot tiles: 1 where the id names row c of the partition's rows."""
                before = sum(len(codes_of) for codes_of in code_list[:u])
                for j, (f, c) in enumerate(code_list[u], start=before):
                    if u == 1 and j - before == CODE_RING + 2:
                        low_fields(0)
                    if u == 0 and j - before >= CODE_RING + 2 and j % 2 == 0 and weights_split < LOOK:
                        low_weights(dve, weights_split)
                        weights_split += 1
                    if j >= CODE_RING:
                        dve.wait_ge(code_used, j - CODE_RING + 1)
                    used, i = splits[f][0], looked_up.index(f)
                    dve.tensor_scalar(codes[0:used, j % CODE_RING, :], ids_wide[0:used, f - low, :], float(c),
                                      first_row_f[0:used, i:i + 1], ALU.subtract, ALU.is_equal).then_inc(
                                          code_ready, 1)

            def multiply(n):
                slot = n % P_RING
                if n >= P_RING:
                    dve.wait_ge(group_reduced, n - P_RING + 1)
                blocks = GROUPS[n][1]
                for s in range(2):
                    m0, m1 = blocks[2 * s][2], blocks[2 * s + 1][2]
                    dve.wait_ge(e_copied, arrival(min(m0, m1)) + 1)
                    dve.wait_ge(step_done, 2 * n + s + 1)
                    if m0 == m1:
                        multiplier = E[:, m0, None, :].to_broadcast([P, 2, BATCH])
                    else:
                        multiplier = E[:, m0:m0 + 2, :]
                    dve.tensor_tensor(prod[:, slot, 2 * s:2 * s + 2, :], ps_t[:, (2 * n + s) % STEPS, :, :], multiplier,
                                      ALU.mult).then_inc(product_ready, 1)

            for u in range(LOOKED_UP):
                encode(u)
            for kind, at in order():
                if kind == "fields":
                    if at:
                        low_fields(at)
                else:
                    if at % 2 == 0 and at // 2 + LOOK < min(NU, DVE_SPLITS):
                        low_weights(dve, at // 2 + LOOK)
                    multiply(at)
            dve.wait_ge(group_reduced, NG)
            top = 32 * (BLOCKS - 1)
            dve.tensor_copy(z[top:top + LAST_ROWS, CHUNKS - 1, :],
                            ps_z[top:top + LAST_ROWS, :]).then_inc(z_tail_copied, 1)

        @block.tensor
        def _(pe):
            def look_up_fields(u):
                before = sum(len(codes_of) for codes_of in code_list[:u])
                for j, (f, c) in enumerate(code_list[u], start=before):
                    if c == 0:
                        pe.wait_ge(small_loaded[f], 16)
                    pe.wait_ge(code_ready, j + 1)
                    half = f % 2 * DIM
                    last = pe.matmul(e_bank[u][half:half + DIM, :], small[f][:, c, :],
                                     codes[0:splits[f][0], j % CODE_RING, :],
                                     start=(c == 0), stop=(c == splits[f][1] - 1)).then_inc(code_used, 1)

            def transpose_fields(u):
                wait_rows(pe, u)
                if u >= 3:
                    pe.wait_ge(low_ready, u if u > 3 else 1)
                for b in range(BT):
                    last = pe.transpose(e_bank[u][:, b * P:(b + 1) * P], rows[:, (u - LOOKED_UP) % G_RING, b, :],
                                        ident[:])
                last.then_inc(transposed, 1)

            def products(n):
                m = n // 2
                pe.wait_ge(w_high_placed, 2 * m + 2)
                pe.wait_ge(w_low_placed[m % W_RING], 32 * (m // W_RING + 1))
                k, blocks = GROUPS[n]
                for s in range(2):
                    step = 2 * n + s
                    if step >= STEPS:
                        pe.wait_ge(product_ready, step - STEPS + 1)
                    for j in range(2):
                        b = 2 * s + j
                        i = blocks[b][0]
                        u = arrival(i // 2)
                        pe.wait_ge(x_loaded[u % X_RING], 64 * (u // X_RING + 1))
                        col = (n % 2 * 2 + b // 2) * P
                        for part in range(2):
                            last = pe.matmul(ps_t[:, step % STEPS, j, :], w_hl[:, m % W_RING, b % 2, col:col + P],
                                             x[:, u % X_RING, i % 2, part, :],
                                             start=(part == 0), stop=(part == 1))
                    last.then_inc(step_done, 1)

            def reduce(n):
                pe.wait_ge(product_ready, 2 * n + 2)
                c, q = divmod(n, PER_CHUNK)
                if c >= 1 and q == 0:
                    pe.wait_ge(z_copied, c)
                at = 2 * (PER_CHUNK - 1 - q)
                for b in range(BLOCKS):
                    last = pe.matmul(ps_z[32 * b:32 * b + 32, :], halves[:, at:at + 32],
                                     prod[:, n % P_RING, b, :], start=(q == 0),
                                     stop=(q == PER_CHUNK - 1 or n == NG - 1))
                last.then_inc(group_reduced, 1)

            pe.wait_ge(ident_ready, 1)
            pe.wait_ge(halves_ready, 2)
            for kind, at in order():
                if kind == "fields":
                    look_up_fields(at) if at < LOOKED_UP else transpose_fields(at)
                else:
                    products(at)
                    if at >= LAG:
                        reduce(at - LAG)

            for n in range(NG - LAG, NG - 1):
                reduce(n)
            pe.wait_ge(params_loaded, 16 * (CHUNKS + 5))
            pe.wait_ge(z_copied, CHUNKS - 1)
            pe.wait_ge(low_ready, KP)

            def sum_h1(m, c0, c1):
                for c in range(c0, c1):
                    used = DENSE_AT + DENSE if c == CHUNKS - 1 else P
                    last = pe.matmul(h1_bank[m], w1_sb[0:used, c, m * P:(m + 1) * P], z[0:used, c, :],
                                     start=(c == 0), stop=(c == CHUNKS - 1))
                return last

            for m in range(3):
                sum_h1(m, 0, CHUNKS - 1)
            reduce(NG - 1)
            for m in range(3, H1 // P):
                sum_h1(m, 0, CHUNKS - 1)
            pe.wait_ge(z_copied, CHUNKS)
            pe.wait_ge(z_tail_copied, 1)
            for m in range(H1 // P):
                sum_h1(m, CHUNKS - 1, CHUNKS).then_inc(h1_summed, 1)
            for c in range(H1 // P):
                pe.wait_ge(h1_ready, c + 1)
                for m in range(H2 // P):
                    last = pe.matmul(h2_bank[m], w2_sb[:, c, m * P:(m + 1) * P], h1[:, c, :],
                                     start=(c == 0), stop=(c == H1 // P - 1))
                    if c == H1 // P - 1:
                        last.then_inc(h2_summed, 1)
            for c in range(H2 // P):
                pe.wait_ge(h2_ready, c + 1)
                last = pe.matmul(y_bank[0:1, :], w3_sb[:, c:c + 1], h2[:, c, :],
                                 start=(c == 0), stop=(c == H2 // P - 1))
            last.then_inc(y_summed, 1)


def z_rows():
    at = np.full((CHUNKS, P), -1)
    for n, (_, blocks) in enumerate(GROUPS):
        for b, (_, halves, _) in enumerate(blocks):
            for h, p in enumerate(halves):
                if p is not None:
                    at[n // PER_CHUNK, 32 * b + 2 * (n % PER_CHUNK) + h] = p
    at[CHUNKS - 1, DENSE_AT:DENSE_AT + DENSE] = PAIRS + np.arange(DENSE)
    return at


def kernel(**inputs):
    from concourse import bacc
    from concourse.bass_utils import run_bass_kernel_spmd

    a = {k: np.asarray(v) for k, v in inputs.items()}
    f32 = a["L0_rec_W"].dtype

    w = np.concatenate([a["L0_rec_W"], np.zeros((1, DIM, DIM), f32)])
    rows = [[[PAIRS if p is None else p for p in halves] for _, halves, _ in blocks] for _, blocks in GROUPS]
    w_units = w[np.array(rows).reshape(NU, 2, 2, 2, 2)].transpose(0, 3, 5, 1, 2, 4, 6)
    w1 = np.concatenate([a["W_top1"], np.zeros((1, H1), f32)])[z_rows()]
    arrays = {
        "w_units": w_units.reshape(NU, P, 2 * BLOCKS // 2 * P),
        "ids_t": a["ids"].reshape(BT, P, FIELDS).transpose(1, 2, 0).reshape(P, FIELDS * BT),
        "ids_by_field": a["ids"].T,
        "dense_t": a["dense_ctx"].T,
        "w1": w1,
        "b1": a["b_top1"].reshape(H1 // P, P).T,
        "w2": a["W_top2"].reshape(H1 // P, P, H2).transpose(1, 0, 2),
        "b2": a["b_top2"].reshape(H2 // P, P).T,
        "w3": a["W_top3"].reshape(H2 // P, P).T,
    }
    for f in range(FIELDS):
        arrays[f"tbl_{f}"] = a[f"tbl_{f}"]
    arrays = {f"in_{k}": np.ascontiguousarray(v) for k, v in arrays.items()}

    nc = bacc.Bacc("TRN2", target_bir_lowering=False, num_devices=1)
    ap = {k: nc.dram_tensor(k, v.shape, mybir.dt.from_np(v.dtype), kind="ExternalInput").ap()
          for k, v in arrays.items()}
    out = nc.dram_tensor("out_y", (1, BATCH), F32, kind="ExternalOutput").ap()
    tower_kernel(nc, ap["in_w_units"], ap["in_ids_t"], ap["in_ids_by_field"], [ap[f"in_tbl_{f}"] for f in range(FIELDS)],
                 ap["in_dense_t"], ap["in_w1"], ap["in_b1"], ap["in_w2"], ap["in_b2"], ap["in_w3"], out)
    r = run_bass_kernel_spmd(nc, [arrays], core_ids=[0])
    return r.results[0]["out_y"].reshape(BATCH, 1)
```

```python
from contextlib import ExitStack

import numpy as np

import concourse.bass as bass
from concourse import mybir

F32 = mybir.dt.float32
F32R = mybir.dt.float32r
I32 = mybir.dt.int32
ALU = mybir.AluOpType
ACT = mybir.ActivationFunctionType

P = 128
BATCH = 512
BT = BATCH // P
FIELDS = 40
DIM = 64
DENSE = 16
PAIRS = FIELDS * (FIELDS - 1) // 2
KP = FIELDS // 2
QUADS = KP // 2
H1, H2 = 512, 256

BLOCKS = 4
PER_CHUNK = 16
LOOKED_UP = 2
CODE_RING = 7
FETCHED_AT = (0, 16)
WEIGHTS_AT = (0, 3)
PARTS_RING = 5
X_RING = 5
G_RING = 4
W_RING = 4
RAW_RING = 4
P_RING = 4
DVE_SPLITS = 33
STEPS = 3
LOOK = 3


def pair(i, j):
    return i * FIELDS - i * (i + 1) // 2 + j - i - 1


def plan_groups():
    groups = []
    for k in reversed(range(KP)):
        for M in range(k // 2 + 1, QUADS):
            groups.append((k, [(i, (pair(i, 2 * m), pair(i, 2 * m + 1)), m)
                               for m in (2 * M, 2 * M + 1) for i in (2 * k, 2 * k + 1)]))
        if k % 2 == 0:
            own = [(2 * c, (None, pair(2 * c, 2 * c + 1)), c) for c in (k, k + 1)]
            cross = [(i, (pair(i, 2 * k + 2), pair(i, 2 * k + 3)), k + 1) for i in (2 * k, 2 * k + 1)]
            groups.append((k, own + cross))
    groups.insert(3, groups.pop(0))
    return groups


GROUPS = plan_groups()
NG = len(GROUPS)
NU = NG // 2
CHUNKS = -(-NG // PER_CHUNK)
LAST_ROWS = 2 * (NG - PER_CHUNK * (CHUNKS - 1))
DENSE_AT = 32 * (BLOCKS - 1) + LAST_ROWS

LATE = 2
EARLY_AHEAD = (5, 5, 5, 5, 3, 3, 3, 4, 4, 4, 5)
AHEAD = 5
PARAMS_AT = 12


def arrival(k):
    return KP - 1 - k


def first_group(u):
    return next((n for n, (k, _) in enumerate(GROUPS) if arrival(k) >= u), NG)


def uses(u):
    return [n for n, (_, blocks) in enumerate(GROUPS) if any(arrival(i // 2) == u for i, _, _ in blocks)]


SPLIT_FIRST = (0, 2, 3, 1)
FIRST = len(SPLIT_FIRST)


def place(u):
    return SPLIT_FIRST.index(u) if u < FIRST else u


def order(late=0):
    u = 0
    for n in range(NG):
        while u < KP and first_group(u) - (AHEAD - late if u >= len(EARLY_AHEAD) else EARLY_AHEAD[u]) <= n:
            yield "fields", u
            u += 1
        yield "group", n


def table_split(rows):
    used = max(d for d in range(1, P + 1) if rows % d == 0)
    return used, rows // used


def tower_kernel(nc, w_units, ids, ids_by_field, tables, dense, w1, b1, w2, b2, w3, out):
    with ExitStack() as ctx:
        def sb(name, shape, dt=F32):
            return ctx.enter_context(nc.sbuf_tensor(name, shape, dt))

        def ps(name, shape, dt=F32):
            return ctx.enter_context(nc.psum_tensor(name, shape, dt))

        def sem(name):
            return ctx.enter_context(nc.semaphore(name))

        ids_sb = sb("ids_sb", [P, FIELDS * BT], I32)
        ident = sb("ident", [P, P])
        looked_up = [2 * (KP - 1 - u) + f for u in range(LOOKED_UP) for f in range(2)]
        splits = {f: table_split(tables[f].shape[0]) for f in looked_up}
        first_row = sb("first_row", [P, len(looked_up)], I32)
        first_row_f = sb("first_row_f", [P, len(looked_up)])
        halves = sb("halves", [P, 2 * (2 * PER_CHUNK - 1)])
        rows = sb("rows", [P, G_RING, BT, 2 * DIM])
        E = sb("E", [P, KP, BATCH])
        parts = sb("parts", [P, PARTS_RING, 2, BATCH], F32R)
        x = sb("x", [P, X_RING, 2, 2, BATCH], F32R)
        w_raw = sb("w_raw", [P, RAW_RING, BLOCKS * P])
        w_high = sb("w_high", [P, 2, BLOCKS * P], F32R)
        w_low = sb("w_low", [P, 2, BLOCKS * P], F32R)
        w_hl = sb("w_hl", [P, W_RING, 2, BLOCKS * P], F32R)
        prod = sb("prod", [P, P_RING, BLOCKS, BATCH])
        scratch = prod[:].rearrange("p a b n -> p (a b n)")
        small, at = {}, 0
        for f in looked_up:
            used, c = splits[f]
            small[f] = scratch[0:used, at:at + c * DIM].rearrange("p (c n) -> p c n", c=c)
            at += c * DIM
        ids_wide = scratch[:, at:at + len(looked_up) * BATCH].bitcast(I32).rearrange(
            "p (f n) -> p f n", f=len(looked_up))
        at += len(looked_up) * BATCH
        codes = scratch[:, at:at + CODE_RING * BATCH].rearrange(
            "p (c n) -> p c n", c=CODE_RING)
        z = sb("z", [P, CHUNKS, BATCH])
        w1_sb = sb("w1_sb", [P, CHUNKS, H1])
        w2_sb = sb("w2_sb", [P, H1 // P, H2])
        w3_sb = sb("w3_sb", [P, H2 // P])
        b1_sb = sb("b1_sb", [P, H1 // P])
        b2_sb = sb("b2_sb", [P, H2 // P])
        y_sb = sb("y_sb", [1, BATCH])
        h1 = E[:, 0:H1 // P, :]
        h2 = E[:, H1 // P:H1 // P + H2 // P, :]

        ps_t = ps("ps_t", [P, STEPS, 2, BATCH])
        ps_e = ps("ps_e", [P, BATCH])
        ps_z = ps("ps_z", [P, BATCH])
        free = [(2 * NG + s) % STEPS for s in range(STEPS)]
        h1_bank = [ps_e[:], ps_t[:, free[0], 0, :], ps_t[:, free[0], 1, :], ps_t[:, free[1], 0, :]]
        h2_bank = [ps_t[:, free[1], 1, :], ps_t[:, free[2], 0, :]]
        y_bank = ps_t[:, free[2], 1, :]
        e_bank = [ps_e[:], ps_t[:, STEPS - 1, 0, :], ps_t[:, STEPS - 1, 1, :]] + [ps_e[:]] * (KP - 3)

        ids_loaded = sem("ids_loaded")
        params_loaded = sem("params_loaded")
        wide_loaded = [sem(f"wide_loaded{u}") for u in range(LOOKED_UP)]
        small_loaded = {f: sem(f"small_loaded{f}") for f in looked_up}
        first_row_ready = sem("first_row_ready")
        first_row_cast = sem("first_row_cast")
        code_ready = sem("code_ready")
        code_used = sem("code_used")
        ident_zeroed = sem("ident_zeroed")
        ident_ready = sem("ident_ready")
        halves_zeroed = sem("halves_zeroed")
        halves_ready = sem("halves_ready")
        rows_loaded = [sem(f"rows_loaded{i}") for i in range(G_RING)]
        transposed = sem("transposed")
        e_copied = sem("e_copied")
        high_ready = sem("high_ready")
        low_ready = sem("low_ready")
        x_loaded = [sem(f"x_loaded{i}") for i in range(X_RING)]
        raw_loaded = [sem(f"raw_loaded{i}") for i in range(RAW_RING)]
        w_high_ready = sem("w_high_ready")
        w_high_placed = sem("w_high_placed")
        w_low_dve = sem("w_low_dve")
        w_low_pool = sem("w_low_pool")
        w_low_placed = [sem(f"w_low_placed{i}") for i in range(W_RING)]
        step_done = sem("step_done")
        product_ready = sem("product_ready")
        group_reduced = sem("group_reduced")
        z_copied = sem("z_copied")
        z_tail_copied = sem("z_tail_copied")
        h1_summed = sem("h1_summed")
        h1_ready = sem("h1_ready")
        h2_summed = sem("h2_summed")
        h2_ready = sem("h2_ready")
        y_summed = sem("y_summed")
        y_ready = sem("y_ready")
        stored = sem("stored")

        code_list = [[(f, c) for c in range(max(splits[f][1] for f in looked_up[2 * u:2 * u + 2]))
                      for f in looked_up[2 * u:2 * u + 2] if c < splits[f][1]] for u in range(LOOKED_UP)]

        def wait_low(eng, m):
            if m < DVE_SPLITS:
                eng.wait_ge(w_low_dve, m + 1)
            else:
                eng.wait_ge(w_low_pool, m + 1 - DVE_SPLITS)

        def wait_rows(eng, u):
            g = u - LOOKED_UP
            eng.wait_ge(rows_loaded[g % G_RING], 16 * 2 * BT * (g // G_RING + 1))

        def low_weights(eng, m):
            eng.wait_ge(w_high_ready, m + 1)
            if m >= 2:
                eng.wait_ge(w_low_placed[(m - 2) % W_RING], 32 * ((m - 2) // W_RING + 1))
            eng.tensor_tensor(w_low[:, m % 2, :], w_raw[:, m % RAW_RING, :], w_high[:, m % 2, :],
                              ALU.subtract).then_inc(w_low_dve if m < DVE_SPLITS else w_low_pool, 1)

        block = ctx.enter_context(nc.Block())

        @block.sync
        def _(sp):
            sp.dma_start(ids_sb[:], ids).then_inc(ids_loaded, 16)
            for u in range(LOOKED_UP):
                sp.dma_start(ids_wide[:, 2 * u:2 * u + 2, :], ids_by_field[None, looked_up[2 * u]:looked_up[2 * u] + 2, :].
                             to_broadcast([P, 2, BATCH])).then_inc(wide_loaded[u], 16)
                for f in looked_up[2 * u:2 * u + 2]:
                    sp.dma_start(small[f], tables[f].rearrange("(p c) n -> p c n", p=splits[f][0])).then_inc(
                        small_loaded[f], 16)

            def load_params():
                for c in range(CHUNKS):
                    sp.dma_start(w1_sb[:, c, :], w1[c]).then_inc(params_loaded, 16)
                sp.dma_start(z[DENSE_AT:DENSE_AT + DENSE, CHUNKS - 1, :], dense).then_inc(params_loaded, 16)
                sp.dma_start(w2_sb[:], w2).then_inc(params_loaded, 16)
                sp.dma_start(w3_sb[:], w3).then_inc(params_loaded, 16)
                sp.dma_start(b1_sb[:], b1).then_inc(params_loaded, 16)
                sp.dma_start(b2_sb[:], b2).then_inc(params_loaded, 16)

            def load_weights(m):
                if m >= RAW_RING:
                    wait_low(sp, m - RAW_RING)
                    sp.wait_ge(w_high_placed, 2 * (m - RAW_RING) + 2)
                sp.dma_start(w_raw[:, m % RAW_RING, :], w_units[m]).then_inc(raw_loaded[m % RAW_RING], 16)

            def place_low(m):
                wait_low(sp, m)
                if m >= W_RING:
                    sp.wait_ge(step_done, 4 * (m - W_RING) + 4)
                for odd, (src, dst) in enumerate(((0, DIM), (DIM, 0))):
                    sp.dma_start(w_hl[dst:dst + DIM, m % W_RING, odd, :].bitcast(F32),
                                 w_low[src:src + DIM, m % 2, :].bitcast(F32)).then_inc(
                                     w_low_placed[m % W_RING], 16)

            def spread_parts(u):
                if u >= X_RING:
                    sp.wait_ge(step_done, 2 * max(uses(u - X_RING)) + 2)
                sp.wait_ge(high_ready, place(u) + 1)
                sp.wait_ge(low_ready, place(u) + 1)
                for f in range(2):
                    for half in (0, DIM):
                        sp.dma_start(x[half:half + DIM, u % X_RING, f, :, :].bitcast(F32),
                                     parts[f * DIM:(f + 1) * DIM, u % PARTS_RING, :, :].bitcast(F32)).then_inc(
                                         x_loaded[u % X_RING], 16)

            for m in range(RAW_RING):
                load_weights(m)
            for m in range(2):
                place_low(m)
                load_weights(m + RAW_RING)
            for u in SPLIT_FIRST:
                spread_parts(u)
            for m in range(2, LOOK):
                place_low(m)
                load_weights(m + RAW_RING)
            for kind, at in order(LATE):
                if kind == "fields":
                    if at >= FIRST:
                        spread_parts(at)
                    if at == PARAMS_AT:
                        load_params()
                elif at % 2 == 0 and at // 2 + LOOK < NU:
                    place_low(at // 2 + LOOK)
                    if at // 2 + LOOK + RAW_RING < NU:
                        load_weights(at // 2 + LOOK + RAW_RING)
            sp.wait_ge(y_ready, 1)
            sp.dma_start(out, y_sb[:]).then_inc(stored, 16)
            sp.wait_ge(stored, 16)

        @block.gpsimd
        def _(pool):
            pool.memset(ident[:], 0.0).then_inc(ident_zeroed, 1)
            pool.wait_ge(ident_zeroed, 1)
            pool.affine_select(out=ident[:], in_=ident[:], compare_op=ALU.not_equal, fill=1.0, base=0,
                               pattern=[[-1, P]], channel_multiplier=1).then_inc(ident_ready, 1)
            for i, f in enumerate(looked_up):
                pool.iota(first_row[:, i:i + 1], pattern=[[0, 1]], base=0,
                          channel_multiplier=splits[f][1]).then_inc(first_row_ready, 1)
            pool.wait_ge(ids_loaded, 16)

            def gather(u):
                k = KP - 1 - u
                g = u - LOOKED_UP
                if g >= G_RING:
                    pool.wait_ge(transposed, g - G_RING + 1)
                for f in range(2):
                    for b in range(BT):
                        col = (2 * k + f) * BT + b
                        pool.indirect_dma_start(
                            rows[:, g % G_RING, b, f * DIM:(f + 1) * DIM], None, tables[2 * k + f],
                            bass.IndirectOffsetOnAxis(ap=ids_sb[:, col:col + 1], axis=0),
                        ).then_inc(rows_loaded[g % G_RING], 16)

            for u in range(LOOKED_UP, KP):
                gather(u)
            wait_rows(pool, KP - 1)
            for m in range(DVE_SPLITS, NU):
                low_weights(pool, m)

        @block.scalar
        def _(act):
            def high_weights(m):
                act.wait_ge(raw_loaded[m % RAW_RING], 16 * (m // RAW_RING + 1))
                if m >= 2:
                    wait_low(act, m - 2)
                act.activation(w_high[:, m % 2, :], w_raw[:, m % RAW_RING, :], ACT.Copy).then_inc(w_high_ready, 1)
                if m >= W_RING:
                    act.wait_ge(step_done, 4 * (m - W_RING) + 4)
                for odd, at in enumerate((0, DIM)):
                    act.activation(w_hl[at:at + DIM, m % W_RING, odd, :], w_raw[at:at + DIM, m % RAW_RING, :],
                                   ACT.Copy).then_inc(w_high_placed, 1)

            def split_fields(u):
                if u < LOOKED_UP:
                    act.wait_ge(code_used, sum(len(codes_of) for codes_of in code_list[:u + 1]))
                else:
                    act.wait_ge(transposed, u - LOOKED_UP + 1)
                act.activation(E[:, KP - 1 - u, :], e_bank[u], ACT.Copy).then_inc(e_copied, 1)
                old = u - PARTS_RING
                if old >= 0:
                    act.wait_ge(x_loaded[old % X_RING], 64 * (old // X_RING + 1))
                act.activation(parts[:, u % PARTS_RING, 0, :], e_bank[u], ACT.Copy).then_inc(high_ready, 1)

            def copy_z(c):
                if c < CHUNKS - 1:
                    act.wait_ge(group_reduced, PER_CHUNK * (c + 1))
                    act.activation(z[:, c, :], ps_z[:], ACT.Copy).then_inc(z_copied, 1)
                else:
                    act.wait_ge(group_reduced, NG)
                    top = 32 * (BLOCKS - 1)
                    act.activation(z[0:top, c, :], ps_z[0:top, :], ACT.Copy).then_inc(z_copied, 1)

            for m in range(2):
                high_weights(m)
            for u in SPLIT_FIRST:
                split_fields(u)
            for m in range(2, LOOK):
                high_weights(m)
            for kind, at in order():
                if kind == "fields":
                    if at >= FIRST:
                        split_fields(at)
                elif kind == "group":
                    if at % 2 == 0 and at // 2 + LOOK < NU:
                        high_weights(at // 2 + LOOK)
                    if at and at % PER_CHUNK == 0:
                        copy_z(at // PER_CHUNK - 1)
            copy_z(CHUNKS - 1)
            act.wait_ge(params_loaded, 16 * (CHUNKS + 5))
            for m in range(H1 // P):
                act.wait_ge(h1_summed, m + 1)
                act.activation(h1[:, m, :], h1_bank[m], ACT.Relu, bias=b1_sb[:, m:m + 1]).then_inc(h1_ready, 1)
            for m in range(H2 // P):
                act.wait_ge(h2_summed, m + 1)
                act.activation(h2[:, m, :], h2_bank[m], ACT.Relu, bias=b2_sb[:, m:m + 1]).then_inc(h2_ready, 1)
            act.wait_ge(y_summed, 1)
            act.activation(y_sb[:], y_bank[0:1, :], ACT.Copy).then_inc(y_ready, 1)

        @block.vector
        def _(dve):
            dve.memset(halves[:], 0.0).then_inc(halves_zeroed, 1)
            mid = 2 * (PER_CHUNK - 1)
            dve.wait_ge(halves_zeroed, 1)
            dve.memset(halves[0:DIM, mid:mid + 1], 1.0).then_inc(halves_ready, 1)
            dve.memset(halves[DIM:P, mid + 1:mid + 2], 1.0).then_inc(halves_ready, 1)

            dve.wait_ge(first_row_ready, len(looked_up))
            dve.tensor_copy(first_row_f[:], first_row[:]).then_inc(first_row_cast, 1)
            dve.wait_ge(first_row_cast, 1)

            def low_fields(u):
                dve.wait_ge(high_ready, place(u) + 1)
                dve.tensor_tensor(parts[:, u % PARTS_RING, 1, :], E[:, KP - 1 - u, :], parts[:, u % PARTS_RING, 0, :],
                                  ALU.subtract).then_inc(low_ready, 1)

            def encode(u):
                before = sum(len(codes_of) for codes_of in code_list[:u])
                dve.wait_ge(wide_loaded[u], 16)
                for j, (f, c) in enumerate(code_list[u], start=before):
                    if u == 1 and j - before == CODE_RING:
                        for first in SPLIT_FIRST[:2]:
                            low_fields(first)
                    if u == 1 and j - before in WEIGHTS_AT:
                        low_weights(dve, WEIGHTS_AT.index(j - before))
                    if j >= CODE_RING:
                        dve.wait_ge(code_used, j - CODE_RING + 1)
                    used, i = splits[f][0], looked_up.index(f)
                    dve.tensor_scalar(codes[0:used, j % CODE_RING, :], ids_wide[0:used, i, :], float(c),
                                      first_row_f[0:used, i:i + 1], ALU.subtract, ALU.is_equal).then_inc(
                                          code_ready, 1)

            def multiply(n):
                slot = n % P_RING
                if n >= P_RING:
                    dve.wait_ge(group_reduced, n - P_RING + 1)
                blocks = GROUPS[n][1]
                for s in range(2):
                    m0, m1 = blocks[2 * s][2], blocks[2 * s + 1][2]
                    dve.wait_ge(e_copied, max(place(arrival(m)) for m in (m0, m1)) + 1)
                    dve.wait_ge(step_done, 2 * n + s + 1)
                    if m0 == m1:
                        multiplier = E[:, m0, None, :].to_broadcast([P, 2, BATCH])
                    else:
                        multiplier = E[:, m0:m0 + 2, :]
                    dve.tensor_tensor(prod[:, slot, 2 * s:2 * s + 2, :], ps_t[:, (2 * n + s) % STEPS, :, :], multiplier,
                                      ALU.mult).then_inc(product_ready, 1)

            for u in range(LOOKED_UP):
                encode(u)
            for u in SPLIT_FIRST[2:]:
                low_fields(u)
            for m in range(2, LOOK):
                low_weights(dve, m)
            for kind, at in order(LATE):
                if kind == "fields":
                    if at >= FIRST:
                        low_fields(at)
                else:
                    if at % 2 == 0 and at // 2 + LOOK < min(NU, DVE_SPLITS):
                        low_weights(dve, at // 2 + LOOK)
                    multiply(at)
            dve.wait_ge(group_reduced, NG)
            top = 32 * (BLOCKS - 1)
            dve.tensor_copy(z[top:top + LAST_ROWS, CHUNKS - 1, :],
                            ps_z[top:top + LAST_ROWS, :]).then_inc(z_tail_copied, 1)

        @block.tensor
        def _(pe):
            def look_up_fields(u):
                before = sum(len(codes_of) for codes_of in code_list[:u])
                for j, (f, c) in enumerate(code_list[u], start=before):
                    if u == 1 and j - before in FETCHED_AT:
                        transpose_fields(LOOKED_UP + FETCHED_AT.index(j - before))
                    if c == 0:
                        pe.wait_ge(small_loaded[f], 16)
                    pe.wait_ge(code_ready, j + 1)
                    half = f % 2 * DIM
                    last = pe.matmul(e_bank[u][half:half + DIM, :], small[f][:, c, :],
                                     codes[0:splits[f][0], j % CODE_RING, :],
                                     start=(c == 0), stop=(c == splits[f][1] - 1)).then_inc(code_used, 1)

            def transpose_fields(u):
                wait_rows(pe, u)
                if u >= 3:
                    pe.wait_ge(high_ready, u if u > 3 else 1)
                for b in range(BT):
                    last = pe.transpose(e_bank[u][:, b * P:(b + 1) * P], rows[:, (u - LOOKED_UP) % G_RING, b, :],
                                        ident[:])
                last.then_inc(transposed, 1)

            def products(n):
                m = n // 2
                if n % 2 == 0:
                    pe.wait_ge(w_high_placed, 2 * m + 2)
                    pe.wait_ge(w_low_placed[m % W_RING], 32 * (m // W_RING + 1))
                for u in [u for u in range(KP) if uses(u)[0] == n]:
                    pe.wait_ge(x_loaded[u % X_RING], 64 * (u // X_RING + 1))
                blocks = GROUPS[n][1]
                for s in range(2):
                    step = 2 * n + s
                    if step == STEPS - 1:
                        pe.wait_ge(high_ready, FIRST)
                    if step >= STEPS:
                        pe.wait_ge(product_ready, step - STEPS + 1)
                    for j in range(2):
                        b = 2 * s + j
                        i = blocks[b][0]
                        u = arrival(i // 2)
                        col = (n % 2 * 2 + b // 2) * P
                        for part in range(2):
                            last = pe.matmul(ps_t[:, step % STEPS, j, :], w_hl[:, m % W_RING, b % 2, col:col + P],
                                             x[:, u % X_RING, i % 2, part, :],
                                             start=(part == 0), stop=(part == 1))
                    last.then_inc(step_done, 1)

            def reduce(n):
                pe.wait_ge(product_ready, 2 * n + 2)
                c, q = divmod(n, PER_CHUNK)
                if c >= 1 and q == 0:
                    pe.wait_ge(z_copied, c)
                at = 2 * (PER_CHUNK - 1 - q)
                for b in range(BLOCKS):
                    last = pe.matmul(ps_z[32 * b:32 * b + 32, :], halves[:, at:at + 32],
                                     prod[:, n % P_RING, b, :], start=(q == 0),
                                     stop=(q == PER_CHUNK - 1 or n == NG - 1))
                last.then_inc(group_reduced, 1)

            pe.wait_ge(ident_ready, 1)
            pe.wait_ge(halves_ready, 2)
            for u in range(LOOKED_UP):
                look_up_fields(u)
            for kind, at in order():
                if kind == "fields":
                    if at >= FIRST:
                        transpose_fields(at)
                else:
                    products(at)
                    if at and at % 2 == 0:
                        reduce(at - 2)
                        reduce(at - 1)

            reduce(NG - 2)
            pe.wait_ge(params_loaded, 16 * (CHUNKS + 5))
            pe.wait_ge(z_copied, CHUNKS - 1)
            pe.wait_ge(high_ready, KP)

            def sum_h1(m, c0, c1):
                for c in range(c0, c1):
                    used = DENSE_AT + DENSE if c == CHUNKS - 1 else P
                    last = pe.matmul(h1_bank[m], w1_sb[0:used, c, m * P:(m + 1) * P], z[0:used, c, :],
                                     start=(c == 0), stop=(c == CHUNKS - 1))
                return last

            for m in range(3):
                sum_h1(m, 0, CHUNKS - 1)
            reduce(NG - 1)
            for m in range(3, H1 // P):
                sum_h1(m, 0, CHUNKS - 1)
            pe.wait_ge(z_copied, CHUNKS)
            pe.wait_ge(z_tail_copied, 1)
            for m in range(H1 // P):
                sum_h1(m, CHUNKS - 1, CHUNKS).then_inc(h1_summed, 1)
            for c in range(H1 // P):
                pe.wait_ge(h1_ready, c + 1)
                for m in range(H2 // P):
                    last = pe.matmul(h2_bank[m], w2_sb[:, c, m * P:(m + 1) * P], h1[:, c, :],
                                     start=(c == 0), stop=(c == H1 // P - 1))
                    if c == H1 // P - 1:
                        last.then_inc(h2_summed, 1)
            for c in range(H2 // P):
                pe.wait_ge(h2_ready, c + 1)
                last = pe.matmul(y_bank[0:1, :], w3_sb[:, c:c + 1], h2[:, c, :],
                                 start=(c == 0), stop=(c == H2 // P - 1))
            last.then_inc(y_summed, 1)


def z_rows():
    at = np.full((CHUNKS, P), -1)
    for n, (_, blocks) in enumerate(GROUPS):
        for b, (_, halves, _) in enumerate(blocks):
            for h, p in enumerate(halves):
                if p is not None:
                    at[n // PER_CHUNK, 32 * b + 2 * (n % PER_CHUNK) + h] = p
    at[CHUNKS - 1, DENSE_AT:DENSE_AT + DENSE] = PAIRS + np.arange(DENSE)
    return at


def kernel(**inputs):
    from concourse import bacc
    from concourse.bass_utils import run_bass_kernel_spmd

    a = {k: np.asarray(v) for k, v in inputs.items()}
    f32 = a["L0_rec_W"].dtype

    w = np.concatenate([a["L0_rec_W"], np.zeros((1, DIM, DIM), f32)])
    rows = [[[PAIRS if p is None else p for p in halves] for _, halves, _ in blocks] for _, blocks in GROUPS]
    w_units = w[np.array(rows).reshape(NU, 2, 2, 2, 2)].transpose(0, 3, 5, 1, 2, 4, 6)
    w1 = np.concatenate([a["W_top1"], np.zeros((1, H1), f32)])[z_rows()]
    arrays = {
        "w_units": w_units.reshape(NU, P, BLOCKS * P),
        "ids_t": a["ids"].reshape(BT, P, FIELDS).transpose(1, 2, 0).reshape(P, FIELDS * BT),
        "ids_by_field": a["ids"].T,
        "dense_t": a["dense_ctx"].T,
        "w1": w1,
        "b1": a["b_top1"].reshape(H1 // P, P).T,
        "w2": a["W_top2"].reshape(H1 // P, P, H2).transpose(1, 0, 2),
        "b2": a["b_top2"].reshape(H2 // P, P).T,
        "w3": a["W_top3"].reshape(H2 // P, P).T,
    }
    for f in range(FIELDS):
        arrays[f"tbl_{f}"] = a[f"tbl_{f}"]
    arrays = {f"in_{k}": np.ascontiguousarray(v) for k, v in arrays.items()}

    nc = bacc.Bacc("TRN2", target_bir_lowering=False, num_devices=1)
    ap = {k: nc.dram_tensor(k, v.shape, mybir.dt.from_np(v.dtype), kind="ExternalInput").ap()
          for k, v in arrays.items()}
    out = nc.dram_tensor("out_y", (1, BATCH), F32, kind="ExternalOutput").ap()
    tower_kernel(nc, ap["in_w_units"], ap["in_ids_t"], ap["in_ids_by_field"], [ap[f"in_tbl_{f}"] for f in range(FIELDS)],
                 ap["in_dense_t"], ap["in_w1"], ap["in_b1"], ap["in_w2"], ap["in_b2"], ap["in_w3"], out)
    r = run_bass_kernel_spmd(nc, [arrays], core_ids=[0])
    return r.results[0]["out_y"].reshape(BATCH, 1)
```
